# Optimizing a Trainium2 kernel written in Bass

```python
import numpy as np
import jax
import jax.numpy as jnp

def _softmax(x, axis=-1):
    return jax.nn.softmax(x, axis=axis)

def _gelu(x):
    return jax.nn.gelu(x, approximate=True)

def _silu(x):
    return jax.nn.silu(x)

def _sigmoid(x):
    return jax.nn.sigmoid(x)

def _layernorm(x, axis=-1, eps=1e-05):
    m = jnp.mean(x, axis=axis, keepdims=True)
    v = jnp.var(x, axis=axis, keepdims=True)
    return (x - m) / jnp.sqrt(v + eps)

def _scatter_add(tgt, idx, src, axis=0):
    return tgt.at[idx].add(src)

def _segment_sum(src, seg, n):
    return jax.ops.segment_sum(src, seg, n)
kernel_name = 'mk_seq_preln_d2_jaxref_r8_639f72'

def setup_inputs(seed: int=0):
    np.random.seed(seed)
    _w = jnp.asarray

    def _L0_attn_setup():
        import jax, jax.numpy as jnp
        from jax import lax
        import numpy as np
        INPUT_DIM, STATE_DIM, CONV_K, EXPAND = (128, 16, 4, 2)
        INNER = INPUT_DIM * EXPAND
        BATCH, SEQ = (2, 256)
        key = jax.random.key(seed)
        ks = jax.random.split(key, 6)
        x = jax.random.normal(ks[0], (BATCH, SEQ, INPUT_DIM), jnp.float32)
        W_in = jax.random.normal(ks[1], (2 * INNER, INPUT_DIM), jnp.float32) * 0.02
        conv_w = jax.random.normal(ks[2], (INNER, 1, CONV_K), jnp.float32) * 0.1
        conv_b = jnp.zeros((INNER,), jnp.float32)
        A_log = jax.random.normal(ks[3], (INNER, STATE_DIM), jnp.float32)
        D = jnp.ones((INNER,), jnp.float32)
        W_out = jax.random.normal(ks[4], (INPUT_DIM, INNER), jnp.float32) * 0.02
        return {'x': x, 'W_in': W_in, 'conv_w': conv_w, 'conv_b': conv_b, 'A_log': A_log, 'D': D, 'W_out': W_out}
    _L0_attn_in = _L0_attn_setup()

    def _L0_ffn_setup():
        import jax, jax.numpy as jnp
        import numpy as np
        B, S, D_IN, D_OUT, E, GATE_K, TOP_K = (4, 1024, 128, 128, 8, 64, 2)

        def _gate(x, Vg):
            T = x.shape[0]
            xe = jnp.einsum('ti,eir->ter', x, Vg)
            proj = jnp.einsum('ter,eir->tei', xe, Vg)
            residuals = jnp.linalg.norm(x[:, None, :] - proj, axis=-1)
            rw = jax.nn.softmax(-residuals, axis=1)
            thr = 1.0 / E
            mask = rw > thr
            rows = jnp.arange(T)[:, None]
            top1_idx = jnp.argmax(rw, axis=1, keepdims=True)
            top1_mask = jnp.zeros_like(mask).at[rows, top1_idx].set(True)
            mask = jnp.where(jnp.any(mask), mask, top1_mask)
            if TOP_K < E:
                _, topi = jax.lax.top_k(rw, TOP_K)
                topk_mask = jnp.zeros_like(mask).at[rows, topi].set(True)
                mask = mask & topk_mask
            fw = rw * mask.astype(rw.dtype)
            sw = fw.sum(axis=1, keepdims=True)
            sw = jnp.where(sw == 0, jnp.ones_like(sw), sw)
            return fw / sw
        key = jax.random.key(seed)
        ks = jax.random.split(key, 6)
        return {'hidden_states': jax.random.normal(ks[0], (B, S, D_IN), dtype=jnp.float32), 'Wp': jax.random.normal(ks[1], (D_OUT, D_IN), dtype=jnp.float32) * 0.02, 'bp': jax.random.normal(ks[2], (D_OUT,), dtype=jnp.float32) * 0.02, 'We': jax.random.normal(ks[3], (E, D_OUT, D_IN), dtype=jnp.float32) * 0.02, 'be': jax.random.normal(ks[4], (E, D_OUT), dtype=jnp.float32) * 0.02, 'Vg': jax.random.normal(ks[5], (E, D_IN, GATE_K), dtype=jnp.float32) * 0.05}
    _L0_ffn_in = _L0_ffn_setup()

    def _L1_attn_setup():
        import jax, jax.numpy as jnp
        import numpy as np
        D_MODEL, N_HEADS = (128, 16)
        D_H = D_MODEL // N_HEADS
        D_HR = D_H // 2
        D_LATENT = 32
        THETA = 10000.0

        def rope(x, theta=THETA):
            S, d = (x.shape[-2], x.shape[-1])
            inv = theta ** (-jnp.arange(0, d, 2, dtype=jnp.float32) / d)
            ang = jnp.arange(S, dtype=jnp.float32)[:, None] * inv
            cos, sin = (jnp.cos(ang), jnp.sin(ang))
            x1, x2 = (x[..., 0::2], x[..., 1::2])
            r1 = x1 * cos - x2 * sin
            r2 = x1 * sin + x2 * cos
            return jnp.stack([r1, r2], axis=-1).reshape(x.shape)
        key = jax.random.key(seed)
        ks = jax.random.split(key, 9)
        s = lambda fan_in: 1.0 / np.sqrt(fan_in)
        return {'x': jax.random.normal(ks[0], (4, 256, D_MODEL), jnp.float32), 'W_DQ': jax.random.normal(ks[1], (D_MODEL, D_LATENT), jnp.float32) * s(D_MODEL), 'W_UQ': jax.random.normal(ks[2], (D_LATENT, N_HEADS * D_H), jnp.float32) * s(D_LATENT), 'W_QR': jax.random.normal(ks[3], (D_LATENT, N_HEADS * D_HR), jnp.float32) * s(D_LATENT), 'W_DKV': jax.random.normal(ks[4], (D_MODEL, D_LATENT), jnp.float32) * s(D_MODEL), 'W_UK': jax.random.normal(ks[5], (D_LATENT, N_HEADS * D_H), jnp.float32) * s(D_LATENT), 'W_UV': jax.random.normal(ks[6], (D_LATENT, N_HEADS * D_H), jnp.float32) * s(D_LATENT), 'W_KR': jax.random.normal(ks[7], (D_MODEL, D_HR), jnp.float32) * s(D_MODEL), 'W_O': jax.random.normal(ks[8], (N_HEADS * D_H, D_MODEL), jnp.float32) * s(N_HEADS * D_H)}
    _L1_attn_in = _L1_attn_setup()

    def _L1_ffn_setup():
        import jax, jax.numpy as jnp
        import numpy as np
        D_IN, D_HID = (128, 512)

        def _ternary(key, shape):
            return jax.random.randint(key, shape, -1, 2).astype(jnp.float32)

        def _tlin(x, w, s):
            return jnp.einsum('bsi,oi->bso', x, w) * s
        key = jax.random.key(seed)
        ks = jax.random.split(key, 12)
        inv = lambda fan: 1.0 / np.sqrt(fan).astype(np.float32)
        return {'x': jax.random.normal(ks[0], (4, 256, D_IN), dtype=jnp.float32), 'w1_w': _ternary(ks[1], (D_HID, D_IN)), 'w1_s': jax.random.uniform(ks[2], (D_HID,), dtype=jnp.float32) * inv(D_IN), 'w2_w': _ternary(ks[3], (D_HID, D_IN)), 'w2_s': jax.random.uniform(ks[4], (D_HID,), dtype=jnp.float32) * inv(D_IN), 'h1_w': _ternary(ks[5], (D_HID, D_HID)), 'h1_s': jax.random.uniform(ks[6], (D_HID,), dtype=jnp.float32) * inv(D_HID), 'h2_w': _ternary(ks[7], (D_HID, D_HID)), 'h2_s': jax.random.uniform(ks[8], (D_HID,), dtype=jnp.float32) * inv(D_HID), 'w3_w': _ternary(ks[9], (D_IN, D_HID)), 'w3_s': jax.random.uniform(ks[10], (D_IN,), dtype=jnp.float32) * inv(D_HID)}
    _L1_ffn_in = _L1_ffn_setup()
    _d = {'L0_attn_x': _L0_attn_in['x'], 'L0_attn_W_in': _L0_attn_in['W_in'], 'L0_attn_conv_w': _L0_attn_in['conv_w'], 'L0_attn_conv_b': _L0_attn_in['conv_b'], 'L0_attn_A_log': _L0_attn_in['A_log'], 'L0_attn_D': _L0_attn_in['D'], 'L0_attn_W_out': _L0_attn_in['W_out'], 'L0_ffn_Wp': _L0_ffn_in['Wp'], 'L0_ffn_bp': _L0_ffn_in['bp'], 'L0_ffn_We': _L0_ffn_in['We'], 'L0_ffn_be': _L0_ffn_in['be'], 'L0_ffn_Vg': _L0_ffn_in['Vg'], 'L1_attn_W_DQ': _L1_attn_in['W_DQ'], 'L1_attn_W_UQ': _L1_attn_in['W_UQ'], 'L1_attn_W_QR': _L1_attn_in['W_QR'], 'L1_attn_W_DKV': _L1_attn_in['W_DKV'], 'L1_attn_W_UK': _L1_attn_in['W_UK'], 'L1_attn_W_UV': _L1_attn_in['W_UV'], 'L1_attn_W_KR': _L1_attn_in['W_KR'], 'L1_attn_W_O': _L1_attn_in['W_O'], 'L1_ffn_w1_w': _L1_ffn_in['w1_w'], 'L1_ffn_w1_s': _L1_ffn_in['w1_s'], 'L1_ffn_w2_w': _L1_ffn_in['w2_w'], 'L1_ffn_w2_s': _L1_ffn_in['w2_s'], 'L1_ffn_h1_w': _L1_ffn_in['h1_w'], 'L1_ffn_h1_s': _L1_ffn_in['h1_s'], 'L1_ffn_h2_w': _L1_ffn_in['h2_w'], 'L1_ffn_h2_s': _L1_ffn_in['h2_s'], 'L1_ffn_w3_w': _L1_ffn_in['w3_w'], 'L1_ffn_w3_s': _L1_ffn_in['w3_s']}
    _x0 = _d['L0_attn_x']
    _d['L0_attn_x'] = jax.random.normal(jax.random.fold_in(jax.random.key(seed), 1), (16, 512, 128), dtype=_x0.dtype)
    del _x0
    return _d

def reference(L0_attn_x, L0_attn_W_in, L0_attn_conv_w, L0_attn_conv_b, L0_attn_A_log, L0_attn_D, L0_attn_W_out, L0_ffn_Wp, L0_ffn_bp, L0_ffn_We, L0_ffn_be, L0_ffn_Vg, L1_attn_W_DQ, L1_attn_W_UQ, L1_attn_W_QR, L1_attn_W_DKV, L1_attn_W_UK, L1_attn_W_UV, L1_attn_W_KR, L1_attn_W_O, L1_ffn_w1_w, L1_ffn_w1_s, L1_ffn_w2_w, L1_ffn_w2_s, L1_ffn_h1_w, L1_ffn_h1_s, L1_ffn_h2_w, L1_ffn_h2_s, L1_ffn_w3_w, L1_ffn_w3_s):

    def _L0_attn_ref(x, W_in, conv_w, conv_b, A_log, D, W_out):
        import jax, jax.numpy as jnp
        from jax import lax
        import numpy as np
        INPUT_DIM, STATE_DIM, CONV_K, EXPAND = (128, 16, 4, 2)
        INNER = INPUT_DIM * EXPAND
        BATCH, SEQ = (2, 256)
        b, s, _ = x.shape
        inner = W_in.shape[0] // 2
        K = conv_w.shape[-1]
        state = A_log.shape[1]
        xr = x @ W_in.T
        x_ssm, res = (xr[..., :inner], xr[..., inner:])
        xc = jnp.transpose(x_ssm, (0, 2, 1))
        xc = jnp.pad(xc, ((0, 0), (0, 0), (K - 1, 0)))
        xc = lax.conv_general_dilated(xc, conv_w, (1,), 'VALID', feature_group_count=inner, dimension_numbers=('NCH', 'OIH', 'NCH'))
        x_conv = jax.nn.silu(jnp.transpose(xc, (0, 2, 1)) + conv_b)
        delta = jax.nn.softplus(x_conv)
        A = -jnp.exp(A_log)
        A_d = jnp.exp(delta[..., None] * A)
        Bx = x_conv * x_conv

        def step(h, inp):
            a_t, bx_t, c_t = inp
            h = a_t * h + bx_t[..., None]
            y = c_t * jnp.sum(h, axis=-1)
            return (h, y)
        h0 = jnp.zeros((b, inner, state), x.dtype)
        _, ys = lax.scan(step, h0, (jnp.moveaxis(A_d, 1, 0), jnp.moveaxis(Bx, 1, 0), jnp.moveaxis(x_conv, 1, 0)))
        y_ssm = jnp.moveaxis(ys, 0, 1)
        y = y_ssm * jax.nn.silu(res) + D * x_conv
        return y @ W_out.T

    def _L0_ffn_ref(hidden_states, Wp, bp, We, be, Vg):
        import jax, jax.numpy as jnp
        import numpy as np
        B, S, D_IN, D_OUT, E, GATE_K, TOP_K = (4, 1024, 128, 128, 8, 64, 2)

        def _gate(x, Vg):
            T = x.shape[0]
            xe = jnp.einsum('ti,eir->ter', x, Vg)
            proj = jnp.einsum('ter,eir->tei', xe, Vg)
            residuals = jnp.linalg.norm(x[:, None, :] - proj, axis=-1)
            rw = jax.nn.softmax(-residuals, axis=1)
            thr = 1.0 / E
            mask = rw > thr
            rows = jnp.arange(T)[:, None]
            top1_idx = jnp.argmax(rw, axis=1, keepdims=True)
            top1_mask = jnp.zeros_like(mask).at[rows, top1_idx].set(True)
            mask = jnp.where(jnp.any(mask), mask, top1_mask)
            if TOP_K < E:
                _, topi = jax.lax.top_k(rw, TOP_K)
                topk_mask = jnp.zeros_like(mask).at[rows, topi].set(True)
                mask = mask & topk_mask
            fw = rw * mask.astype(rw.dtype)
            sw = fw.sum(axis=1, keepdims=True)
            sw = jnp.where(sw == 0, jnp.ones_like(sw), sw)
            return fw / sw
        in_shape = hidden_states.shape
        pretrained_out = jnp.einsum('bsi,oi->bso', hidden_states, Wp) + bp
        x = hidden_states.reshape(-1, in_shape[-1])
        w = _gate(x, Vg)
        expert_out = jnp.einsum('ti,eoi->teo', x, We) + be[None]
        final = jnp.einsum('te,teo->to', w, expert_out)
        final = final.reshape(*in_shape[:-1], We.shape[1])
        return pretrained_out + final

    def _L1_attn_ref(x, W_DQ, W_UQ, W_QR, W_DKV, W_UK, W_UV, W_KR, W_O):
        import jax, jax.numpy as jnp
        import numpy as np
        D_MODEL, N_HEADS = (128, 16)
        D_H = D_MODEL // N_HEADS
        D_HR = D_H // 2
        D_LATENT = 32
        THETA = 10000.0

        def rope(x, theta=THETA):
            S, d = (x.shape[-2], x.shape[-1])
            inv = theta ** (-jnp.arange(0, d, 2, dtype=jnp.float32) / d)
            ang = jnp.arange(S, dtype=jnp.float32)[:, None] * inv
            cos, sin = (jnp.cos(ang), jnp.sin(ang))
            x1, x2 = (x[..., 0::2], x[..., 1::2])
            r1 = x1 * cos - x2 * sin
            r2 = x1 * sin + x2 * cos
            return jnp.stack([r1, r2], axis=-1).reshape(x.shape)
        B, S, _ = x.shape
        d_qk = D_H + D_HR
        c_q = x @ W_DQ
        Qc = (c_q @ W_UQ).reshape(B, S, N_HEADS, D_H).transpose(0, 2, 1, 3)
        Qr = (c_q @ W_QR).reshape(B, S, N_HEADS, D_HR).transpose(0, 2, 1, 3)
        Qr = rope(Qr)
        c_kv = x @ W_DKV
        Kc = (c_kv @ W_UK).reshape(B, S, N_HEADS, D_H).transpose(0, 2, 1, 3)
        Kr = rope((x @ W_KR)[:, None, :, :])
        Kr = jnp.broadcast_to(Kr, (B, N_HEADS, S, D_HR))
        V = (c_kv @ W_UV).reshape(B, S, N_HEADS, D_H).transpose(0, 2, 1, 3)
        Q = jnp.concatenate([Qc, Qr], axis=-1)
        K = jnp.concatenate([Kc, Kr], axis=-1)
        scores = jnp.einsum('bhqd,bhkd->bhqk', Q, K)
        scores = jnp.clip(scores, -80.0, 80.0)
        causal = jnp.tril(jnp.ones((S, S), dtype=bool))
        scores = jnp.where(causal, scores, -jnp.inf)
        weights = jax.nn.softmax(scores / jnp.sqrt(jnp.float32(d_qk)), axis=-1)
        attn = jnp.einsum('bhqk,bhkd->bhqd', weights, V)
        attn = attn.transpose(0, 2, 1, 3).reshape(B, S, N_HEADS * D_H)
        return attn @ W_O

    def _L1_ffn_ref(x, w1_w, w1_s, w2_w, w2_s, h1_w, h1_s, h2_w, h2_s, w3_w, w3_s):
        import jax, jax.numpy as jnp
        import numpy as np
        D_IN, D_HID = (128, 512)

        def _ternary(key, shape):
            return jax.random.randint(key, shape, -1, 2).astype(jnp.float32)

        def _tlin(x, w, s):
            return jnp.einsum('bsi,oi->bso', x, w) * s
        h = jax.nn.silu(_tlin(x, w1_w, w1_s)) * _tlin(x, w2_w, w2_s)
        h = jax.nn.gelu(_tlin(h, h1_w, h1_s), approximate=False)
        h = jax.nn.gelu(_tlin(h, h2_w, h2_s), approximate=False)
        return _tlin(h, w3_w, w3_s)
    x = L0_attn_x
    x = x + _L0_attn_ref(_layernorm(x, axis=-1), L0_attn_W_in, L0_attn_conv_w, L0_attn_conv_b, L0_attn_A_log, L0_attn_D, L0_attn_W_out)
    x = x + _L0_ffn_ref(_layernorm(x, axis=-1), L0_ffn_Wp, L0_ffn_bp, L0_ffn_We, L0_ffn_be, L0_ffn_Vg)
    x = x + _L1_attn_ref(_layernorm(x, axis=-1), L1_attn_W_DQ, L1_attn_W_UQ, L1_attn_W_QR, L1_attn_W_DKV, L1_attn_W_UK, L1_attn_W_UV, L1_attn_W_KR, L1_attn_W_O)
    x = x + _L1_ffn_ref(_layernorm(x, axis=-1), L1_ffn_w1_w, L1_ffn_w1_s, L1_ffn_w2_w, L1_ffn_w2_s, L1_ffn_h1_w, L1_ffn_h1_s, L1_ffn_h2_w, L1_ffn_h2_s, L1_ffn_w3_w, L1_ffn_w3_s)
    return x

_drawn_inputs = setup_inputs


def setup_inputs(seed=0):
    import zlib

    import numpy as np

    out = dict(_drawn_inputs(seed))
    spreads = {'L0_attn_conv_b': (0.0, 0.1), 'L0_attn_D': (1.0, 0.2)}
    factors = {}
    for name, (base, spread) in spreads.items():
        noise = np.random.default_rng([zlib.crc32(name.encode()), seed]).standard_normal(out[name].shape)
        drawn = base * np.exp(spread * noise) if base else spread * noise
        out[name] = jnp.asarray(drawn.astype(out[name].dtype))
    for name, factor in factors.items():
        out[name] = (out[name] * factor).astype(out[name].dtype)
    return out
```

```python
from contextlib import ExitStack

import concourse.bass as bass
import numpy as np
from concourse import mybir

F32 = mybir.dt.float32
BF16 = mybir.dt.bfloat16
F32R = mybir.dt.float32r
I32 = mybir.dt.int32
ALU = mybir.AluOpType
ACT = mybir.ActivationFunctionType
AX = mybir.AxisListType.X

P = 128
NSEQ, SEQ, DM = 16, 512, 128
NT = SEQ // P
INNER, STATE, TAPS = 256, 16, 4
CT = INNER // P
QUAD = 4
STATE_BUFFERS = 10
NE, GATE_K, TOP_K = 8, 64, 2
HEADS, DH, DR, LAT = 16, 8, 4, 32
DQK = DH + DR
HID = 512
MT = HID // P
EPS = 1e-5
LN_MIN = 1e-19
SCALE = 1.0 / float(np.sqrt(np.float32(DQK)))
CLIP_LO, CLIP_HI = float(np.exp(-80.0 * SCALE)), float(np.exp(80.0 * SCALE))

Q_PART = [0, 1, 2, 0, 1, 0]
K_PART = [0, 0, 0, 1, 1, 2]
Q_RUNS = [(0, 0, 3), (3, 0, 2), (5, 0, 1)]
K_RUNS = [(i, K_PART[i], 1) for i in range(6)]
STACK_ROWS = 96
HALF = HEADS // 2
GROUP = 4
T_TILES = [[0], [1, 3], [2]]
T_COL = {0: 0, 1: 0, 3: 384, 2: 0}
VW = DH + 1
TABLES_EXP_LN, TABLES_GELU = 6, 10
F_IN_FLIGHT = 3
NORMS_MAX = 80.0 ** 2 * 0.98
LEAD = 8


class Mark:

    def __init__(self, sem, value, eta):
        self.sem, self.value, self.eta = sem, value, eta


class Pool:

    def __init__(self, items):
        self.free = [(x, []) for x in items]

    def give_back(self, item, marks):
        self.free.append((item, marks))


class Machine:

    LATENCY, PE_LATENCY, DMA_ISSUE = 135, 300, 500

    def __init__(self, nc, ctx):
        self.nc, self.ctx = nc, ctx
        self.engines = {"sync": nc.sync, "tensor": nc.tensor, "vector": nc.vector, "scalar": nc.scalar,
                        "gpsimd": nc.gpsimd}
        self.clock = dict.fromkeys(self.engines, 0.0)
        self.sems, self.count, self.passed = {}, {}, {}
        self.board = {}

    def sem(self, name):
        if name not in self.sems:
            self.sems[name] = self.ctx.enter_context(self.nc.semaphore(name))
            self.count[name] = 0
        return self.sems[name]

    def start_of(self, engine, after):
        return max([self.clock[engine]] + [
            m.eta + (self.PE_LATENCY if m.sem.startswith("tensor") else self.LATENCY) for m in after])

    def issue(self, engine, cost, stage, fn, after, dma_sem=None):
        start = self.start_of(engine, after)
        eng = self.engines[engine]
        for m in after:
            if self.passed.get((engine, m.sem), 0) < m.value:
                self.passed[engine, m.sem] = m.value
                eng.wait_ge(self.sems[m.sem], m.value)
        name = dma_sem or f"{engine}_{stage}"
        by = 16 if dma_sem else 1
        fn(eng).then_inc(self.sem(name), by)
        self.count[name] += by
        self.clock[engine] = start + (self.DMA_ISSUE if dma_sem else cost)
        return Mark(name, self.count[name], start + cost)

    def join(self, except_for):
        for engine, eng in self.engines.items():
            for name, sem in self.sems.items():
                if not (except_for and name.startswith(except_for)) and self.passed.get((engine, name), 0) < self.count[name]:
                    eng.wait_ge(sem, self.count[name])
                    self.passed[engine, name] = self.count[name]
        self.clock = dict.fromkeys(self.clock, max(self.clock.values()))


def weave(machine, strands):
    live = [[rank, g, None, None] for rank, g in strands]
    for s in live:
        s[2] = next(s[1])
    while live:
        best, best_start = None, None
        for s in live:
            want = s[2]
            while want is not None and want[0] != "step":
                if want[0] == "take":
                    if not want[1].free:
                        break
                    got = want[1].free.pop(0)
                elif want[1] in machine.board:
                    got = machine.board[want[1]]
                else:
                    break
                try:
                    want = s[1].send(got)
                except StopIteration:
                    want = None
            s[2] = want
            if want is None or want[0] != "step":
                continue
            start = machine.start_of(want[1], want[5])
            if best is None or (start, s[0]) < (best_start, best[0]):
                best, best_start = s, start
        live = [s for s in live if s[2] is not None]
        if not live:
            return
        assert best is not None
        try:
            best[2] = best[1].send(machine.issue(*best[2][1:]))
        except StopIteration:
            live.remove(best)


def pe_cost(cols, passes=4):
    return cols * passes / 2.4 + 3


def act_cost(cols, psum=True, pointers=0):
    return (51 if psum else 93) + 93 * pointers + cols / 1.2


def dve_cost(cols, fast=False):
    return 67 + cols / 0.96 / (2 if fast else 1)


def gp_cost(cols):
    return 100 + cols * 2.15


def build(nc, t, stages="SGTF"):
    ctx = ExitStack()
    with ctx:
        mc = Machine(nc, ctx)
        board = mc.board

        def step(engine, cost, stage, fn, after, dma=None):
            return ("step", engine, cost, stage, fn, after) + ((dma,) if dma else ())

        def load(dst, src, key, after=()):
            return step("sync", 2500, "", lambda e: e.dma_start(dst, src), list(after), "load_" + key)

        def allocator(area, tag):
            return lambda name, shape, dt=F32: area.enter_context(nc.sbuf_tensor(f"{name}_{tag}", shape, dt))

        sb = allocator(ctx, "kept")
        banks = Pool([ctx.enter_context(nc.psum_tensor(f"bank{i}", [P, 512], F32)) for i in range(8)])
        x_res = sb("x_res", [P, NSEQ * NT, DM])
        ident = sb("ident", [P, P])
        f_stats = sb("f_stats", [P, NSEQ * NT, 3])
        kept_max = sb("kept_max", [P, NT])
        ones = sb("ones", [P, P])
        kept_sum = sb("kept_sum", [P, 1])
        kept_thr = sb("kept_thr", [P, 2])
        chan_all = sb("chan_all", [P, 3, 4, SEQ])
        w_cols = {"w1_t": HID, "w2_t": HID, "h1_t": MT * HID, "h2_t": MT * HID, "w3_t": MT * DM}
        w_raw, at = {}, 0
        for key, n in w_cols.items():
            w_raw[key] = chan_all[:].rearrange("p a b t -> p (a b t)")[:, at:at + n]
            at += n
        s1, s2 = sb("s1", [P, MT]), sb("s2", [P, MT])
        sh1, sh2 = sb("sh1", [P, MT]), sb("sh2", [P, MT])
        s3_row = sb("s3_row", [P, DM])
        flags = sb("flags", [P, 3])
        go_on = sb("go_on", [1, 1], I32)

        def moments(b, stage, x_ready, raw_pool, stats):
            raw, raw_free = yield ("take", raw_pool)
            marks = []
            for k in range(NT):
                marks.append((yield step("vector", dve_cost(128), stage, lambda e: e.bn_stats(
                    raw[:, k, 0:6], x_res[:, b * NT + k]), x_ready + raw_free)))
            for k in range(NT):
                m = yield step("vector", 75, stage, lambda e: e.bn_aggr(
                    stats[:, k, 0:2], raw[:, k, 0:6]), [marks[k]])
            m = yield step("vector", 75, stage, lambda e: e.tensor_scalar(
                stats[:, :, 1], stats[:, :, 1], EPS, None, ALU.add), [m])
            raw_pool.give_back(raw, [m])
            m = yield step("scalar", 100, stage, lambda e: e.activation(stats[:, :, 2], stats[:, :, 1], ACT.Ln), [m])
            return (yield step("scalar", 100, stage, lambda e: e.activation(
                stats[:, :, 2], stats[:, :, 2], ACT.Exp, scale=-0.5), [m]))

        def turned_norm(b, stage, x_ready, xn_pool, stats_pool=None, raw_pool=None):
            xn, xn_free = yield ("take", xn_pool)
            if stage == "F":
                stats, rstd = f_stats[:, b * NT:(b + 1) * NT], []
            else:
                stats, stats_free = yield ("take", stats_pool)
                rstd = [(yield from moments(b, stage, x_ready + stats_free, raw_pool, stats))]
            marks = []
            for k in range(NT):
                marks.append((yield step("vector", 256, stage, lambda e, k=k: e.tensor_scalar(
                    xn[:, k], x_res[:, b * NT + k], stats[:, k, 0:1], stats[:, k, 2:3],
                    ALU.subtract, ALU.mult), rstd + x_ready + xn_free)))
            if stage != "F":
                stats_pool.give_back(stats, [marks[-1]])
            idm = yield ("read", "ident")
            bank, bank_free = yield ("take", banks)

            def turn(e):
                for k in range(NT):
                    ins = e.transpose(bank[:, k * P:(k + 1) * P], xn[:, k], ident[:])
                return ins
            turned = yield step("tensor", 440, stage, turn, marks + bank_free + idm)
            xn_pool.give_back(xn, [turned])
            return bank, turned

        def layernorm(b, stage, x_ready, xnt_pool, xn_pool, stats_pool, raw_pool):
            xnt, xnt_free = yield ("take", xnt_pool)
            bank, turned = yield from turned_norm(b, stage, x_ready, xn_pool, stats_pool, raw_pool)
            m = yield step("scalar", act_cost(512), stage,
                           lambda e: e.activation(xnt[:], bank[:], ACT.Copy), [turned] + xnt_free)
            banks.give_back(bank, [m])
            return xnt, m

        def phase_one(area, tag, general):
            sb = allocator(area, tag)
            w_in = sb("w_in", [P, 2 * INNER])
            conv_w = sb("conv_w", [P, CT, TAPS])
            conv_b = sb("conv_b", [P, CT])
            a_log = sb("a_log", [P, CT * STATE])
            neg_a = sb("neg_a", [P, CT * STATE])
            skip_d = sb("skip_d", [P, CT])
            w_out = sb("w_out", [P, CT, DM])
            resid_m = sb("resid_m", [P, NE * P])
            we_t = sb("we_t", [P, NE * P])
            wp_t = sb("wp_t", [P, DM])
            bias_e = sb("bias_e", [NE + 1, DM])
            tie = sb("tie", [P, NE, NE])
            lat_w = sb("lat_w", [P, 2 * LAT])
            kr_w = sb("kr_w", [P, 2 * DR])
            up_w = sb("up_w", [2 * LAT, 256])
            rope = sb("rope", [HEADS * DR + DR, 2, SEQ])
            w_o = sb("w_o", [P, DM])
            xn_pool = Pool([sb(f"xn{i}", [P, NT, DM]) for i in range(2)])
            sel_in = sb("sel_in", [P, 64])
            sel = sb("sel", [P, 2, 32], BF16)
            squares_pool = Pool([sb("squares", [P, 3, SEQ], BF16)])
            norms = sb("norms", [2 * 32, NSEQ])
            norms_q = sb("norms_q", [NSEQ, 32])
            xnt_pool = Pool([sb(f"xnt{i}", [P, SEQ]) for i in range(5)])
            stats_pool = Pool([sb(f"ln{i}", [P, NT, 3]) for i in range(4)])
            raw_pool = Pool([sb(f"bn{i}", [P, NT, 6]) for i in range(3)])
            ln_pools = (xnt_pool, xn_pool, stats_pool, raw_pool)
            chan_pool = Pool([chan_all[:, i] for i in range(3)])
            y_all = sb("y_all", [P, 2, SEQ])
            y_pool = Pool([y_all[:, i] for i in range(2)])
            state_pool = Pool([sb(f"state{i}", [P, SEQ]) for i in range(STATE_BUFFERS)])
            gate_pool = Pool([sb(f"gate{i}", [P, 460]) for i in range(2)])
            w9t_pool = Pool([sb("w9t", [NE + 1, SEQ])])
            split_pool = Pool([(sb("parts", [P, 3, 3, SEQ], BF16), sb("latent", [2 * LAT, SEQ]))])
            rest_pool = Pool([sb(f"rest{i}", [P, SEQ]) for i in range(2)])
            v_pool = Pool([sb(f"v_ext{i}", [P, NT, HEADS * VW + 32 - VW]) for i in range(2)])
            stacks = sb("stacks", [P, 2, 2, HALF, SEQ], BF16)
            stack_pool = Pool([(i, stacks[:, i, 0], stacks[:, i, 1]) for i in range(2)])
            probs = [sb(f"prob{i}", [P, GROUP * SEQ]) for i in range(3)]
            vg_t = probs[2][0:GATE_K, 0:NE * P]
            prob_pool = Pool(probs[0:2])
            num_pool = Pool([sb(f"num{i}", [P, SEQ]) for i in range(2)])
            attn_pool = Pool([(sb(f"attn{i}", [P, NT, DM]), sb(f"rden{i}", [P, NT, GROUP])) for i in range(1)])
            def setup_loads():
                for b in range(NSEQ):
                    s = slice(b * NT, b * NT + NT)
                    board["x", b] = [(yield load(x_res[:, s], t["x"][:, s], f"x{b}"))]
                    if b == 0:
                        for key, dst in (("ident", ident[:]), ("w_in", w_in[:]), ("conv_w", conv_w[:]),
                                         ("conv_b", conv_b[:]), ("a_log", a_log[:]), ("skip_d", skip_d[:]),
                                         ("w_out", w_out[:]), ("vg_t", vg_t), ("we_t", we_t[:]),
                                         ("wp_t", wp_t[:]), ("bias_e", bias_e[:]), ("tie", tie[:]),
                                         ("lat_w", lat_w[:]), ("kr_w", kr_w[:]), ("up_w", up_w[:]),
                                         ("rope", rope[:]), ("w_o", w_o[:]), ("sel", sel_in[:])):
                            board[key] = [(yield load(dst, t[key], key))]

            def setup_weights():
                a_in = yield ("read", "a_log")
                m = yield step("scalar", act_cost(32, False), "init",
                               lambda e: e.activation(neg_a[:], a_log[:], ACT.Exp), a_in)
                board["neg_a"] = [(yield step("vector", dve_cost(32), "init",
                                              lambda e: e.tensor_scalar(neg_a[:], neg_a[:], -1.0, None, ALU.mult), [m]))]
                sel_ok = yield ("read", "sel")
                board["sel_bf16"] = [(yield step("vector", 90, "init", lambda e: e.tensor_copy(
                    sel[:].rearrange("p a b -> p (a b)"), sel_in[:]), sel_ok))]
                m = yield step("vector", 8600, "init", lambda e: e.memset(
                    stacks[64:96].rearrange("p s a h t -> p (s a h t)").bitcast(F32), 0.0), [])
                board["stack_zero"] = [m]
                marks = []
                for v, _ in v_pool.free:
                    marks.append((yield step("gpsimd", 900, "init", lambda e, v=v: e.memset(v[:], 1.0), [])))
                board["v_ones"] = marks
                marks = []
                for g, _ in gate_pool.free:
                    marks.append((yield step("gpsimd", 400, "init", lambda e, g=g: e.memset(g[:, 64:100], 1.0), [])))
                board["gate_ones"] = marks
                if not general:
                    yield step("gpsimd", 300, "init", lambda e: e.memset(ones[:], 1.0), [])
                    board["kept_zero"] = [(yield step("gpsimd", 100, "init", lambda e: e.memset(
                        kept_max[:], 0.0), []))]
                    board["flags_zero"] = [(yield step("gpsimd", 100, "init", lambda e: e.memset(flags[:], 0.0), []))]
                vg = yield ("read", "vg_t")
                idm = yield ("read", "ident")
                marks = []
                for half in range(2):
                    bank, free = yield ("take", banks)

                    def outer(e, bank=bank, half=half):
                        for k in range(4):
                            c = slice((half * 4 + k) * P, (half * 4 + k + 1) * P)
                            ins = e.matmul(bank[:, k * P:(k + 1) * P], vg_t[:, c], vg_t[:, c], start=True, stop=True)
                        return ins
                    m = yield step("tensor", pe_cost(512), "init", outer, vg + free)
                    m = yield step("vector", dve_cost(512), "init", lambda e, bank=bank, half=half: e.tensor_tensor(
                        resid_m[:, half * 512:(half + 1) * 512].rearrange("p (a b) -> p a b", b=P),
                        ident[:].unsqueeze(1).to_broadcast([P, 4, P]),
                        bank[:].rearrange("p (a b) -> p a b", b=P), ALU.subtract), idm + [m])
                    banks.give_back(bank, [m])
                    marks.append(m)
                board["resid_m"] = marks
                prob_pool.give_back(probs[2], marks)

            def f_moments(b, x_key):
                board["f_stats", b] = yield from moments(b, "F", (yield ("read", x_key)), raw_pool, f_stats[:, b * NT:(b + 1) * NT])

            def f_loads():
                yield ("read", ("x_S", NSEQ - 1))
                readers = []
                for _ in range(3):
                    readers += (yield ("take", chan_pool))[1]
                for key in w_cols:
                    board["raw", key] = [(yield load(w_raw[key], t[key], key, readers))]
                for key, dst in (("s1", s1), ("s2", s2), ("sh1", sh1), ("sh2", sh2), ("s3_row", s3_row)):
                    board[key] = [(yield load(dst[:], t[key], key))]

            def s_head(b):
                if b >= LEAD and "T" in stages:
                    yield ("read", ("x_T", b - LEAD))
                xnt, ready = yield from layernorm(b, "S", (yield ("read", ("x", b))), *ln_pools)
                board["s_xnt", b] = (xnt, ready)
                reads = []
                for ct in range(CT):
                    reads += yield ("read", ("s_read", b, ct))
                xnt_pool.give_back(xnt, reads)

            def sigmoid(out, v, psum, after):
                m = yield step("vector", dve_cost(512, not psum), "S",
                               lambda e: e.tensor_scalar(out, v, -40.0, None, ALU.max), after)
                m = yield step("scalar", act_cost(512, False), "S",
                               lambda e: e.activation(out, out, ACT.Exp, scale=-1.0), [m])
                m = yield step("scalar", act_cost(512, False), "S",
                               lambda e: e.activation(out, out, ACT.Ln, bias=1.0), [m])
                return (yield step("scalar", act_cost(512, False), "S",
                                   lambda e: e.activation(out, out, ACT.Exp, scale=-1.0), [m]))

            def s_channels(b, ct):
                xnt, ready = yield ("read", ("s_xnt", b))
                w_ok = (yield ("read", "w_in")) + (yield ("read", "conv_w")) + (yield ("read", "conv_b"))
                if (b, ct) != (0, 0):
                    yield ("read", ("s_began", (CT * b + ct - 1) // CT, (ct - 1) % CT))
                chan, chan_free = yield ("take", chan_pool)
                board["s_began", b, ct] = True
                xc, delta, bx, gate = [chan[:, i] for i in range(4)]
                tmp = delta
                bank, free = yield ("take", banks)
                proj = yield step("tensor", pe_cost(512), "S", lambda e: e.matmul(
                    bank[:], w_in[:, ct * P:(ct + 1) * P], xnt[:], start=True, stop=True), [ready] + w_ok + free)
                m = yield step("scalar", act_cost(512, True, 2), "S", lambda e: e.activation(
                    tmp, bank[:], ACT.Identity, bias=conv_b[:, ct:ct + 1],
                    scale=conv_w[:, ct, TAPS - 1:TAPS]), [proj] + chan_free)
                for back in range(1, TAPS):
                    m = yield step("vector", dve_cost(512), "S", lambda e, back=back: e.scalar_tensor_tensor(
                        out=tmp[:, back:], in0=bank[:, 0:SEQ - back],
                        scalar=conv_w[:, ct, TAPS - 1 - back:TAPS - back], in1=tmp[:, back:],
                        op0=ALU.mult, op1=ALU.add), [m])
                banks.give_back(bank, [m])
                m = yield from sigmoid(xc, tmp, False, [m])
                xc_ok = yield step("gpsimd", gp_cost(512), "S", lambda e: e.tensor_tensor(xc, tmp, xc, ALU.mult), [m])
                m = yield step("scalar", act_cost(512, False), "S",
                               lambda e: e.activation(tmp, xc, ACT.Exp, scale=-1.0), [xc_ok])
                m = yield step("scalar", act_cost(512, False), "S",
                               lambda e: e.activation(tmp, tmp, ACT.Ln, bias=1.0), [m])
                bx_ok = yield step("gpsimd", gp_cost(512), "S",
                                   lambda e: e.tensor_tensor(bx, xc, xc, ALU.mult), [xc_ok])
                delta_ok = yield step("gpsimd", gp_cost(512), "S",
                                      lambda e: e.tensor_tensor(delta, tmp, xc, ALU.add), [m])
                board["s_scan", b, ct] = (chan, delta_ok, bx_ok)
                bank2, free = yield ("take", banks)
                col = (CT + ct) * P
                proj2 = yield step("tensor", pe_cost(512), "S", lambda e: e.matmul(
                    bank2[:], w_in[:, col:col + P], xnt[:], start=True, stop=True), free)
                board["s_read", b, ct] = [proj, proj2]
                m = yield from sigmoid(gate, bank2[:], True, [proj2])
                gate_ok = yield step("vector", dve_cost(512), "S", lambda e: e.tensor_tensor(
                    gate, bank2[:], gate, ALU.mult), [m])
                banks.give_back(bank2, [gate_ok])
                state_bank, summed = yield ("read", ("s_summed", b, ct))
                m = yield step("vector", dve_cost(512), "S", lambda e: e.tensor_tensor(
                    gate, state_bank[:], gate, ALU.mult), [summed, gate_ok])
                banks.give_back(state_bank, [m])
                d_ok = yield ("read", "skip_d")
                y, y_free = yield ("take", y_pool)
                y_ok = yield step("vector", dve_cost(512), "S", lambda e: e.scalar_tensor_tensor(
                    out=y, in0=gate, scalar=skip_d[:, ct:ct + 1], in1=xc, op0=ALU.add, op1=ALU.mult), [m] + d_ok + y_free)
                chan_pool.give_back(chan, [y_ok])
                board["s_y", b, ct] = (y, y_ok)

            def s_decay(b, ct):
                a_ok = yield ("read", "neg_a")
                chan, delta_ok, _ = yield ("read", ("s_scan", b, ct))
                for n in range(STATE):
                    h, free = yield ("take", state_pool)
                    c = ct * STATE + n
                    m = yield step("scalar", act_cost(512, False, 1), "S", lambda e: e.activation(
                        h[:], chan[:, 1], ACT.Exp, scale=neg_a[:, c:c + 1]), [delta_ok] + a_ok + free)
                    board["s_decay", b, ct, n] = (h, m)

            def s_scan(b, ct):
                chan, _, bx_ok = yield ("read", ("s_scan", b, ct))
                for n in range(STATE):
                    h, ready = yield ("read", ("s_decay", b, ct, n))
                    m = yield step("vector", dve_cost(512), "S", lambda e: e.tensor_tensor_scan(
                        h[:], h[:], chan[:, 2], 0.0, ALU.mult, ALU.add), [ready, bx_ok])
                    board["s_hist", b, ct, n] = (h, m)

            def s_sum(b, ct):
                yield ("read", ("s_hist", b, ct, 0))
                bank, free = yield ("take", banks)
                for first in range(0, STATE, QUAD):
                    hs, ms = [], []
                    for n in range(first, first + QUAD):
                        h, m = yield ("read", ("s_hist", b, ct, n))
                        hs.append(h)
                        ms.append(m)
                        if n % 2:
                            ms[-2] = yield step("gpsimd", gp_cost(512), "S", lambda e: e.tensor_tensor(
                                hs[-2][:], hs[-2][:], hs[-1][:], ALU.add), ms[-2:])
                            state_pool.give_back(hs[-1], [ms[-2]])
                    m = yield step("gpsimd", gp_cost(512), "S", lambda e: e.tensor_tensor(
                        hs[0][:], hs[0][:], hs[2][:], ALU.add), [ms[0], ms[2]])
                    state_pool.give_back(hs[2], [m])
                    m = yield step("tensor", pe_cost(512), "S", lambda e: e.matmul(
                        bank[:], ident[:], hs[0][:], start=(first == 0), stop=(first == STATE - QUAD)), [m] + free)
                    state_pool.give_back(hs[0], [m])
                board["s_summed", b, ct] = (bank, m)

            def s_out(b):
                ys = []
                for ct in range(CT):
                    ys.append((yield ("read", ("s_y", b, ct))))
                w_ok = yield ("read", "w_out")
                bank, free = yield ("take", banks)

                def project(e):
                    for k in range(NT):
                        for ct in range(CT):
                            ins = e.matmul(bank[:, k * P:(k + 1) * P], ys[ct][0][:, k * P:(k + 1) * P],
                                           w_out[:, ct], start=(ct == 0), stop=(ct == CT - 1))
                    return ins
                m = yield step("tensor", pe_cost(1024), "S", project, [y for _, y in ys] + w_ok + free)
                for y, _ in ys:
                    y_pool.give_back(y, [m])
                yield from residual(b, "S", bank, m)

            def residual(b, stage, bank, m):
                s = slice(b * NT, b * NT + NT)
                m = yield step("vector", dve_cost(512), stage, lambda e: e.tensor_tensor(
                    x_res[:, s], bank[:].rearrange("p (k f) -> p k f", k=NT), x_res[:, s], ALU.add), [m])
                banks.give_back(bank, [m])
                board["x_" + stage, b] = [m]

            def g_all(b, x_key):
                xnt, ready = yield from layernorm(b, "G", (yield ("read", x_key)), *ln_pools)
                m_ok, we_ok = (yield ("read", "resid_m")), (yield ("read", "we_t"))
                gb, g_free = yield ("take", gate_pool)
                ones_ok = yield ("read", "gate_ones")
                ss = gb[:, 0:32].rearrange("p (k e) -> p k e", k=NT)
                rw = gb[:, 32:64].rearrange("p (k e) -> p k e", k=NT)
                w9 = gb[:, 64:100].rearrange("p (k e) -> p k e", k=NT)
                rank = gb[:, 100:132].rearrange("p (k e) -> p k e", k=NT)
                fw = gb[:, 132:164].rearrange("p (k e) -> p k e", k=NT)
                col = lambda i: gb[:, 164 + 4 * i:168 + 4 * i]
                diff = gb[:, 200:456].rearrange("p (k e j) -> p k e j", k=NT, e=NE)

                def over_e(c):
                    return c.unsqueeze(2).to_broadcast([P, NT, NE])
                marks = []
                for k in range(NT):
                    for half in range(2):
                        bank, free = yield ("take", banks)
                        m = yield step("tensor", pe_cost(512), "G", lambda e: e.matmul(
                            bank[:], xnt[:, k * P:(k + 1) * P], resid_m[:, half * 512:(half + 1) * 512],
                            start=True, stop=True), [ready] + m_ok + free)
                        m = yield step("scalar", act_cost(512), "G", lambda e: e.activation(
                            bank[:], bank[:], ACT.Square), [m])
                        m = yield step("vector", dve_cost(512), "G", lambda e: e.tensor_reduce(
                            ss[:, k, half * 4:half * 4 + 4], bank[:].rearrange("p (a b) -> p a b", b=P), AX, ALU.add),
                            [m] + g_free)
                        banks.give_back(bank, [m])
                        marks.append(m)
                v = lambda cost, fn, after: step("vector", cost, "G", fn, after)
                m = yield v(90, lambda e: e.tensor_scalar(ss, ss, LN_MIN, None, ALU.max), [marks[-1]])
                m = yield step("scalar", 130, "G", lambda e: e.activation(ss, ss, ACT.Ln), [m])
                m = yield step("scalar", 130, "G", lambda e: e.activation(ss, ss, ACT.Exp, scale=0.5), [m])
                m = yield v(90, lambda e: e.tensor_reduce(col(0), ss, AX, ALU.min), [m])
                m = yield v(90, lambda e: e.tensor_tensor(ss, ss, over_e(col(0)), ALU.subtract), [m])
                m = yield step("scalar", 130, "G", lambda e: e.activation(ss, ss, ACT.Exp, scale=-1.0), [m])
                m = yield v(90, lambda e: e.tensor_reduce(col(1), ss, AX, ALU.add), [m])
                m = yield v(90, lambda e: e.reciprocal(col(2), col(1)), [m])
                m = yield v(90, lambda e: e.tensor_tensor(rw, ss, over_e(col(2)), ALU.mult), [m])
                rw_ok = m
                tie_ok = yield ("read", "tie")
                m = yield v(340, lambda e: e.tensor_tensor(
                    diff, rw.unsqueeze(2).to_broadcast([P, NT, NE, NE]),
                    rw.unsqueeze(3).to_broadcast([P, NT, NE, NE]), ALU.subtract), [m])
                m = yield v(340, lambda e: e.tensor_tensor(
                    diff, diff, tie[:].unsqueeze(1).to_broadcast([P, NT, NE, NE]), ALU.is_gt), [m] + tie_ok)
                m = yield v(340, lambda e: e.tensor_reduce(rank, diff, AX, ALU.add), [m])
                thr = kept_thr[:, 0:1] if general else 1.0 / NE
                limit = kept_thr[:, 1:2] if general else TOP_K - 0.5
                m2 = yield v(90, lambda e: e.scalar_tensor_tensor(
                    out=fw, in0=rw, scalar=thr, in1=rw, op0=ALU.is_gt, op1=ALU.mult), [rw_ok])
                m = yield v(90, lambda e: e.scalar_tensor_tensor(
                    out=fw, in0=rank, scalar=limit, in1=fw, op0=ALU.is_lt, op1=ALU.mult), [m, m2])
                m = yield v(90, lambda e: e.tensor_reduce(col(3), fw, AX, ALU.add), [m])
                if not general:
                    kept_prev = [(yield ("read", ("g_kept", b - 1)))] if b else (yield ("read", "kept_zero"))
                    board["g_kept", b] = yield v(90, lambda e: e.tensor_tensor(
                        kept_max[:], kept_max[:], col(3), ALU.max), [m] + kept_prev)
                m = yield v(90, lambda e: e.scalar_tensor_tensor(
                    out=col(4), in0=col(3), scalar=0.0, in1=col(3), op0=ALU.is_equal, op1=ALU.add), [m])
                m = yield v(90, lambda e: e.reciprocal(col(5), col(4)), [m])
                w_ok = yield v(90, lambda e: e.tensor_tensor(
                    w9[:, :, 0:NE], fw, over_e(col(5)), ALU.mult), [m] + ones_ok)
                bank, free = yield ("take", banks)

                def turn(e):
                    for k in range(NT):
                        ins = e.transpose(bank[0:NE + 1, k * P:(k + 1) * P], w9[:, k], ident[:])
                    return ins
                turned = yield step("tensor", 440, "G", turn, [w_ok] + free)
                w9t, w9t_free = yield ("take", w9t_pool)
                w9t_ok = yield step("scalar", act_cost(512), "G", lambda e: e.activation(
                    w9t[:], bank[0:NE + 1, :], ACT.Copy), [turned] + w9t_free)
                banks.give_back(bank, [w9t_ok])
                wp_ok, be_ok = (yield ("read", "wp_t")), (yield ("read", "bias_e"))
                bank, free = yield ("take", banks)

                def shared(e):
                    for k in range(NT):
                        c = slice(k * P, (k + 1) * P)
                        e.matmul(bank[:, c], xnt[:, c], wp_t[:], start=True, stop=False)
                        ins = e.matmul(bank[:, c], w9t[:, c], bias_e[:], start=False, stop=True)
                    return ins
                m = yield step("tensor", pe_cost(1024), "G", shared, [w9t_ok] + wp_ok + be_ok + free)
                w9t_pool.give_back(w9t, [m])
                s = slice(b * NT, b * NT + NT)
                m = yield step("vector", dve_cost(512), "G", lambda e, bank=bank: e.tensor_tensor(
                    x_res[:, s], bank[:].rearrange("p (k f) -> p k f", k=NT), x_res[:, s], ALU.add), [m])
                banks.give_back(bank, [m])
                last = [m] * NT
                for half in range(2):
                    for k in range(NT):
                        bank, free = yield ("take", banks)
                        mm = yield step("tensor", pe_cost(512), "G", lambda e: e.matmul(
                            bank[:], xnt[:, k * P:(k + 1) * P], we_t[:, half * 512:(half + 1) * 512],
                            start=True, stop=True), we_ok + free)
                        for i in range(4):
                            ex = half * 4 + i
                            last[k] = yield step("vector", dve_cost(190), "G", lambda e, bank=bank: e.scalar_tensor_tensor(
                                out=x_res[:, b * NT + k], in0=bank[:, i * P:(i + 1) * P],
                                scalar=w9[:, k, ex:ex + 1], in1=x_res[:, b * NT + k],
                                op0=ALU.mult, op1=ALU.add), [mm, last[k]])
                        banks.give_back(bank, [last[k]])
                xnt_pool.give_back(xnt, [mm])
                gate_pool.give_back(gb, last)
                board["x_G", b] = last

            def t_project(b, x_key):
                xnt, ready = yield from layernorm(b, "T", (yield ("read", x_key)), *ln_pools)
                lat_ok = (yield ("read", "lat_w")) + (yield ("read", "kr_w")) + (yield ("read", "up_w"))
                (parts, latent), split_free = yield ("take", split_pool)
                bank, free = yield ("take", banks)
                m = yield step("tensor", pe_cost(512), "T", lambda e: e.matmul(
                    bank[0:2 * LAT, :], lat_w[:], xnt[:], start=True, stop=True), [ready] + lat_ok + free)
                lat = yield step("scalar", act_cost(512), "T", lambda e, bank=bank: e.activation(
                    latent[:], bank[0:2 * LAT, :], ACT.Copy), [m] + split_free)
                banks.give_back(bank, [lat])
                cq, ckv = latent[0:LAT], latent[LAT:2 * LAT]
                v_ext, v_free = yield ("take", v_pool)
                v_ones = yield ("read", "v_ones")
                bank, free = yield ("take", banks)

                def values(e, bank=bank):
                    for k in range(NT):
                        ins = e.matmul(bank[:, k * P:(k + 1) * P], ckv[:, k * P:(k + 1) * P],
                                       up_w[LAT:2 * LAT, P:2 * P], start=True, stop=True, tile_position=(LAT, 0))
                    return ins
                m = yield step("tensor", pe_cost(512), "T", values, [lat] + free)
                m = yield step("vector", dve_cost(512), "T", lambda e, bank=bank: e.tensor_scalar(
                    v_ext[:, :, 0:HEADS * VW].rearrange("p k (h c) -> p k h c", c=VW)[:, :, :, 0:DH],
                    bank[:].rearrange("p (k h c) -> p k h c", k=NT, c=DH), 1.0, None, ALU.mult), [m] + v_free + v_ones)
                banks.give_back(bank, [m])
                board["t_v", b] = (v_ext, m)

                def split(i, rows, src, after):
                    p0 = yield step("scalar", act_cost(512), "T", lambda e: e.activation(
                        parts[0:rows, i, 0], src, ACT.Copy), after)
                    rest, rest_free = yield ("take", rest_pool)
                    r = yield step("vector", dve_cost(512), "T", lambda e: e.tensor_tensor(
                        rest[0:rows], src, parts[0:rows, i, 0], ALU.subtract), [p0] + rest_free)
                    p1 = yield step("scalar", act_cost(512, False), "T", lambda e: e.activation(
                        parts[0:rows, i, 1], rest[0:rows], ACT.Copy), [r])
                    p2 = yield step("gpsimd", gp_cost(470), "T", lambda e: e.tensor_tensor(
                        parts[0:rows, i, 2], rest[0:rows], parts[0:rows, i, 1], ALU.subtract), [p1])
                    rest_pool.give_back(rest, [p2])
                    return [p0, p1, p2], r
                done, squared = [], []
                if not general:
                    squares, sq_free = yield ("take", squares_pool)
                for i, row in enumerate((0, LAT)):
                    bank, free = yield ("take", banks)
                    m = yield step("tensor", pe_cost(512), "T", lambda e: e.matmul(
                        bank[:], up_w[row:row + LAT, 0:P], latent[row:row + LAT], start=True, stop=True,
                        tile_position=(row, 0)), free)
                    sq_done = []
                    if not general:
                        sq_done = [(yield step("scalar", act_cost(512), "T", lambda e, bank=bank: e.activation(
                            squares[:, i], bank[:], ACT.Square), [m] + sq_free))]
                        squared += sq_done
                    d, read = yield from split(i, P, bank[:], [m])
                    banks.give_back(bank, [read] + sq_done)
                    done += d
                rope_ok = yield ("read", "rope")
                nq, rows = HEADS * DR, HEADS * DR + DR
                turned = []
                for swap in range(2):
                    bank, free = yield ("take", banks)

                    def rotary(e, bank=bank):
                        e.matmul(bank[0:nq, :], up_w[0:LAT, P + swap * nq:P + (swap + 1) * nq], cq, start=True, stop=True, tile_position=(0, 0))
                        return e.matmul(bank[nq:rows, :], kr_w[:, swap * DR:(swap + 1) * DR], xnt[:],
                                        start=True, stop=True, tile_position=(0, nq))
                    m = yield step("tensor", pe_cost(512), "T", rotary, free)
                    last_read = m
                    rest, rest_free = yield ("take", rest_pool)
                    m = yield step("vector", dve_cost(512), "T", lambda e, bank=bank: e.tensor_tensor(
                        rest[0:rows], bank[0:rows, :], rope[:, swap], ALU.mult), [m] + rope_ok + rest_free)
                    banks.give_back(bank, [m])
                    turned.append((rest, m))
                xnt_pool.give_back(xnt, [last_read])
                (a, am), (c, cm) = turned
                m = yield step("gpsimd", gp_cost(512), "T", lambda e: e.tensor_tensor(
                    a[0:rows], a[0:rows], c[0:rows], ALU.add), [am, cm])
                rest_pool.give_back(c, [m])
                if not general:
                    squared.append((yield step("scalar", act_cost(512, False), "T", lambda e: e.activation(
                        squares[0:rows, 2], a[0:rows], ACT.Square), [m])))
                    sel_ok = yield ("read", "sel_bf16")
                    bank, free = yield ("take", banks)

                    def sums(e, bank=bank):
                        e.matmul(bank[0:32, :], sel[:, 0], squares[:, 0], start=True, stop=False, tile_position=(0, 0))
                        e.matmul(bank[0:32, :], sel[0:nq, 1], squares[0:nq, 2], start=False, stop=True,
                                 tile_position=(0, 0))
                        e.matmul(bank[32:64, :], sel[:, 0], squares[:, 1], start=True, stop=False, tile_position=(0, 32))
                        return e.matmul(bank[32:64, :], sel[nq:rows, 1], squares[nq:rows, 2], start=False, stop=True,
                                        tile_position=(nq, 32))
                    n = yield step("tensor", pe_cost(2048, 1), "T", sums, squared + sel_ok + free)
                    squares_pool.give_back(squares, [n])
                    n = yield step("vector", dve_cost(512), "T", lambda e, bank=bank: e.tensor_reduce(
                        norms[:, b:b + 1], bank[0:64, :], AX, ALU.max), [n])
                    banks.give_back(bank, [n])
                    board["t_norms", b] = n
                    squared = squared[-1:]
                d, read = yield from split(2, rows, a[0:rows], [m])
                rest_pool.give_back(a, [read] + d + squared)
                done += d
                for part in range(3):
                    r = part * DQK
                    for rows_to, tile, first in (("q_rows", 0, 0), ("k_rows", 1, nq)):
                        out = t[rows_to][b]
                        m = yield step("sync", 2500, "T", lambda e: e.dma_start(
                            out[:, r:r + DH], parts[:, tile, part]), done, "rows")
                        if first == 0:
                            m = yield step("sync", 2500, "T", lambda e: e.dma_start(
                                out[:, r + DH:r + DQK], parts[0:nq, 2, part]), done, "rows")
                        else:
                            m = yield step("sync", 2500, "T", lambda e: e.dma_start(
                                out[:, r + DH:r + DQK].rearrange("h c t -> c h t"),
                                parts[nq:rows, 2, part].unsqueeze(1).to_broadcast([DR, HEADS, SEQ])), done, "rows")
                written = m
                split_pool.give_back((parts, latent), [written])
                zero_ok = yield ("read", "stack_zero")
                for half in range(2):
                    (slot, kst, qst), free = yield ("take", stack_pool)
                    heads = slice(half * HALF, (half + 1) * HALF)
                    for dst, rows_from, runs in ((qst, "q_rows", Q_RUNS), (kst, "k_rows", K_RUNS)):
                        for block, part, n in runs:
                            m = yield step("sync", 2500, "T", lambda e: e.dma_start(
                                dst[DQK * block:DQK * (block + n)],
                                t[rows_from][b, heads, DQK * part:DQK * (part + n)].rearrange("h r t -> r h t")),
                                [written] + free + zero_ok, f"stack{slot}")
                    board["t_stack", b, half] = (slot, kst, qst, m)

            def t_bound():
                marks = []
                for b in range(NSEQ):
                    marks.append((yield ("read", ("t_norms", b))))
                bank, free = yield ("take", banks)
                m = yield step("tensor", 200, "T", lambda e: e.transpose(
                    bank[0:NSEQ, 0:64], norms[:], ident[0:64, 0:64]), marks + free)
                m = yield step("vector", 90, "T", lambda e: e.tensor_copy(norms_q[:], bank[0:NSEQ, 0:32]), [m])
                m = yield step("vector", 90, "T", lambda e: e.tensor_tensor(
                    norms_q[:, 0:HEADS], norms_q[:, 0:HEADS], bank[0:NSEQ, 32:32 + HEADS], ALU.mult), [m])
                banks.give_back(bank, [m])
                m = yield step("vector", 90, "T", lambda e: e.tensor_scalar(
                    norms_q[:, 0:HEADS], norms_q[:, 0:HEADS], NORMS_MAX, None, ALU.is_lt), [m])
                m = yield step("vector", 90, "T", lambda e: e.tensor_reduce(
                    norms_q[:, HEADS:HEADS + 1], norms_q[:, 0:HEADS], AX, ALU.min), [m])
                zero = yield ("read", "flags_zero")
                yield step("vector", 90, "T", lambda e: e.tensor_scalar(
                    flags[0:NSEQ, 2:3], norms_q[:, HEADS:HEADS + 1], -1.0, 1.0, ALU.mult, ALU.add), [m] + zero)

            def t_scores(b, half):
                slot, kst, qst, stacked = yield ("read", ("t_stack", b, half))
                reads = []
                for grp in range(HALF // GROUP):
                    heads = [grp * GROUP + j for j in range(GROUP)]
                    for kind, tiles in enumerate(T_TILES):
                        prob, p_free = yield ("take", prob_pool)
                        if kind < 2:
                            work = [[(h, kt, T_COL[kt]) for kt in tiles] for h in heads]
                        else:
                            work = [[(heads[2 * i], 2, 0), (heads[2 * i + 1], 2, 256)] for i in range(2)]
                        exps, pending = [], []

                        def finish():
                            i, bank, m = pending.pop(0)
                            m = yield step("scalar", act_cost(512), "T", lambda e: e.activation(
                                prob[:, i * 512:(i + 1) * 512], bank[:], ACT.Exp, scale=SCALE), [m] + p_free)
                            banks.give_back(bank, [m])
                            exps.append(m)
                        for i, pieces in enumerate(work):
                            bank, free = yield ("take", banks)

                            def multiply(e, bank=bank, pieces=pieces):
                                for h, kt, c in pieces:
                                    ins = e.matmul(bank[:, c:c + SEQ - P * kt],
                                                   kst[0:STACK_ROWS, h, P * kt:P * kt + P],
                                                   qst[0:STACK_ROWS, h, P * kt:SEQ], start=True, stop=True)
                                return ins
                            m = yield step("tensor", pe_cost(512, 1), "T", multiply, [stacked] + free)
                            pending.append((i, bank, m))
                            if len(pending) == 2:
                                yield from finish()
                        while pending:
                            yield from finish()
                        reads.append(m)
                        board["t_prob", b, half, grp, kind] = (prob, exps)
                stack_pool.give_back((slot, kst, qst), [reads[-1]])

            def t_values(b, half):
                v_ext, v_ok = yield ("read", ("t_v", b))
                for grp in range(HALF // GROUP):
                    yield ("read", ("t_prob", b, half, grp, 0))
                    bank, free = yield ("take", banks)
                    for kind, tiles in enumerate(T_TILES):
                        prob, exps = yield ("read", ("t_prob", b, half, grp, kind))
                        width = 2048 if kind < 2 else 1024
                        ready = exps
                        if general:
                            m = yield step("vector", dve_cost(width, True), "T", lambda e: e.tensor_scalar(
                                prob[:, 0:width], prob[:, 0:width], CLIP_LO, CLIP_HI, ALU.max, ALU.min), exps)
                            ready = [m]
                        per = width // GROUP
                        for kt in tiles:
                            blocks = prob[:, 0:width].rearrange("p (j c) -> p j c", j=GROUP)[:, :, T_COL[kt]:T_COL[kt] + P]
                            m = yield step("gpsimd", 540, "T", lambda e, blocks=blocks: e.affine_select(
                                out=blocks, in_=blocks, compare_op=ALU.is_ge, fill=0.0, base=0,
                                pattern=[[0, GROUP], [1, P]], channel_multiplier=-1), ready)
                            ready = [m]

                        def weigh(e):
                            for kt in tiles:
                                for j in range(GROUP):
                                    h = half * HALF + grp * GROUP + j
                                    c = j * per + T_COL[kt]
                                    ins = e.matmul(bank[32 * j:32 * j + 32, P * kt:SEQ],
                                                   v_ext[:, kt, h * VW:h * VW + 32], prob[:, c:c + SEQ - P * kt],
                                                   start=(kt == 0), stop=(kt == 2), tile_position=(0, 32 * j),
                                                   skip_group_check=True)
                            return ins
                        m = yield step("tensor", pe_cost(width, 1), "T", weigh, [m, v_ok] + free)
                        prob_pool.give_back(prob, [m])
                    board["t_num", b, half * 2 + grp] = (bank, m)
                board["t_v_read", b, half] = [m]

            def t_finish(b):
                yield ("read", ("t_num", b, 0))
                (attn, rden), a_free = yield ("take", attn_pool)
                marks = []
                for g in range(HEADS // GROUP):
                    pv, m = yield ("read", ("t_num", b, g))
                    num, n_free = yield ("take", num_pool)
                    m = yield step("scalar", act_cost(512), "T", lambda e: e.activation(num[:], pv[:], ACT.Copy),
                                   [m] + n_free)
                    banks.give_back(pv, [m])
                    bank, free = yield ("take", banks)

                    def turn(e):
                        for k in range(NT):
                            ins = e.transpose(bank[:, k * P:(k + 1) * P], num[:, k * P:(k + 1) * P], ident[:])
                        return ins
                    m = yield step("tensor", 440, "T", turn, [m] + free)
                    num_pool.give_back(num, [m])
                    rows = bank[:].rearrange("p (k j c) -> p k j c", k=NT, c=32)
                    m = yield step("vector", 170, "T", lambda e: e.reciprocal(
                        rden[:].unsqueeze(3), rows[:, :, :, DH:DH + 1]), [m] + a_free + marks[-1:])
                    m = yield step("vector", 200, "T", lambda e: e.tensor_tensor(
                        attn[:, :, g * 32:(g + 1) * 32].rearrange("p k (j c) -> p k j c", c=DH),
                        rows[:, :, :, 0:DH], rden[:].unsqueeze(3).to_broadcast([P, NT, GROUP, DH]), ALU.mult), [m])
                    banks.give_back(bank, [m])
                    marks.append(m)
                v_ext, _ = yield ("read", ("t_v", b))
                v_pool.give_back(v_ext, (yield ("read", ("t_v_read", b, 0))) + (yield ("read", ("t_v_read", b, 1))))
                bank, free = yield ("take", banks)

                def turn_back(e):
                    for k in range(NT):
                        ins = e.transpose(bank[:, k * P:(k + 1) * P], attn[:, k], ident[:])
                    return ins
                m = yield step("tensor", 440, "T", turn_back, marks + free)
                attn_pool.give_back((attn, rden), [m])
                num, n_free = yield ("take", num_pool)
                m = yield step("scalar", act_cost(512), "T", lambda e: e.activation(num[:], bank[:], ACT.Copy), [m] + n_free)
                banks.give_back(bank, [m])
                wo_ok = yield ("read", "w_o")
                bank, free = yield ("take", banks)

                def project(e):
                    for k in range(NT):
                        c = slice(k * P, (k + 1) * P)
                        ins = e.matmul(bank[:, c], num[:, c], w_o[:], start=True, stop=True)
                    return ins
                m = yield step("tensor", pe_cost(512), "T", project, [m] + wo_ok + free)
                num_pool.give_back(num, [m])
                yield from residual(b, "T", bank, m)

            strands = [(0, setup_loads()), (0, setup_weights())]
            for b in range(NSEQ):
                key = ("x", b)
                r = 10 * b
                if "S" in stages:
                    strands += [(r + 5, s_head(b)), (r + 5, s_out(b))]
                    for ct in range(CT):
                        strands += [(r + 5, f(b, ct)) for f in (s_sum, s_scan, s_decay, s_channels)]
                    key = ("x_S", b)
                if "G" in stages:
                    strands.append((r + 2, g_all(b, key)))
                    key = ("x_G", b)
                if "T" in stages:
                    strands += [(r + 0, t_finish(b)), (r + 1, t_project(b, key))]
                    for half in range(2):
                        strands += [(r, t_values(b, half)), (r + 1, t_scores(b, half))]
                    key = ("x_T", b)
                strands.append((r + 1, f_moments(b, key)))
            if "T" in stages and not general:
                strands.append((0, t_bound()))
            if "F" in stages:
                strands.append((0, f_loads()))
            weave(mc, [(0, tables(TABLES_EXP_LN))])
            weave(mc, strands)

        def phase_two(area, tag, general):
            sb = allocator(area, tag)
            dt = F32 if general else F32R
            PARTS = 1 if general else 2
            w, at = dict(w_raw), 0
            if not general:
                w_all = sb("w_all", [P, sum(w_cols.values())], F32R)
                for key, n in w_cols.items():
                    w[key] = w_all[:, at:at + n]
                    at += n
            unequal = sb("unequal", [P, len(w_cols)])
            s1_half, s12_half = sb("s1_half", [P, MT]), sb("s12_half", [P, MT])
            xn_pool = Pool([sb(f"xn{i}", [P, NT, DM]) for i in range(2)])
            xnt_pool = Pool([sb(f"xnt{i}", [P, PARTS, SEQ], dt) for i in range(3)])
            hid_pool = Pool([sb(f"hid{i}", [P, PARTS, SEQ], dt) for i in range(8 * F_IN_FLIGHT - 1)])
            tmp_pool = Pool([sb(f"tmp{i}", [P, SEQ]) for i in range(6)])
            out_pool = Pool([(i, sb(f"out{i}", [P, NT, DM])) for i in range(2)])

            def f_weights():
                a, b2 = (yield ("read", "s1")), (yield ("read", "s2"))
                m1 = yield step("vector", 80, "F",
                                lambda e: e.tensor_scalar(s1_half[:], s1[:], 0.5, None, ALU.mult), a)
                m2 = yield step("vector", 80, "F", lambda e: e.scalar_tensor_tensor(
                    out=s12_half[:], in0=s1[:], scalar=0.5, in1=s2[:], op0=ALU.mult, op1=ALU.mult), b2)
                board["f_scales"] = [m1, m2]
                if general:
                    for key in w_cols:
                        board[key] = board["raw", key]
                    return
                for key, n in w_cols.items():
                    ok = yield ("read", ("raw", key))
                    board[key] = [(yield step("vector", dve_cost(n, True), "F", lambda e: e.tensor_copy(
                        w[key], w_raw[key]), ok))]

            def f_compare():
                marks = []
                for i, (key, n) in enumerate(w_cols.items()):
                    rounded = yield ("read", key)
                    yield ("read", ("f_done", 2 + i))
                    m = yield step("vector", dve_cost(n), "F", lambda e: e.tensor_tensor(
                        w_raw[key], w_raw[key], w[key].bitcast(F32), ALU.not_equal), rounded)
                    marks.append((yield step("vector", dve_cost(n), "F", lambda e: e.tensor_reduce(
                        unequal[:, i:i + 1], w_raw[key], AX, ALU.max), [m])))
                board["f_unequal"] = (yield step("vector", 90, "F", lambda e: e.tensor_reduce(
                    flags[:, 1:2], unequal[:], AX, ALU.max), [marks[-1]]))

            def low_part(dst, src, engine, after):
                cost = gp_cost(512) if engine == "gpsimd" else dve_cost(512)
                return step(engine, cost, "F", lambda e: e.tensor_tensor(
                    dst[:, 1], src, dst[:, 0].bitcast(F32), ALU.subtract), after)

            def f_all(b):
                xnt, xnt_free = yield ("take", xnt_pool)
                bank, turned = yield from turned_norm(b, "F", [], xn_pool)
                m = yield step("scalar", act_cost(512), "F", lambda e, bank=bank: e.activation(
                    xnt[:, 0], bank[:], ACT.Copy), [turned] + xnt_free)
                ready = [m]
                if not general:
                    m = yield low_part(xnt, bank[:], "vector", [m])
                    ready.append(m)
                banks.give_back(bank, [m])
                w_ok = (yield ("read", "w1_t")) + (yield ("read", "w2_t")) + (yield ("read", "f_scales"))
                passes = 4 if general else 2
                if b >= F_IN_FLIGHT:
                    yield ("read", ("f_last_layer", b - F_IN_FLIGHT))
                h, tiles = [], []
                for mt in range(MT):
                    c = slice(mt * P, (mt + 1) * P)

                    def project(e, key, bank):
                        for i in range(PARTS):
                            ins = e.matmul(bank[:], w[key][:, c], xnt[:, i], start=(i == 0), stop=(i == PARTS - 1))
                        return ins
                    bank, free = yield ("take", banks)
                    m = yield step("tensor", pe_cost(512, passes), "F",
                                   lambda e, bank=bank: project(e, "w1_t", bank), ready + w_ok + free)
                    th, th_free = yield ("take", tmp_pool)
                    m = yield step("scalar", act_cost(512, True, 1), "F", lambda e, bank=bank: e.activation(
                        th[:], bank[:], ACT.Tanh, scale=s1_half[:, mt:mt + 1]), [m] + w_ok + th_free)
                    m = yield step("vector", dve_cost(512), "F", lambda e, bank=bank: e.scalar_tensor_tensor(
                        out=th[:], in0=th[:], scalar=1.0, in1=bank[:], op0=ALU.add, op1=ALU.mult), [m])
                    banks.give_back(bank, [m])
                    bank, free = yield ("take", banks)
                    m2 = yield step("tensor", pe_cost(512, passes), "F",
                                    lambda e, bank=bank: project(e, "w2_t", bank), free)
                    cell, cell_free = yield ("take", hid_pool)
                    out = cell[:, 0] if general else th[:]
                    m = yield step("vector", dve_cost(512), "F", lambda e, bank=bank: e.scalar_tensor_tensor(
                        out=out, in0=bank[:], scalar=s12_half[:, mt:mt + 1], in1=th[:],
                        op0=ALU.mult, op1=ALU.mult), [m, m2] + (cell_free if general else []))
                    banks.give_back(bank, [m])
                    if not general:
                        hi = yield step("scalar", act_cost(512, False), "F", lambda e: e.activation(
                            cell[:, 0], th[:], ACT.Copy), [m] + cell_free)
                        m = yield low_part(cell, th[:], "gpsimd" if mt else "vector", [hi])
                        tiles.append(hi)
                    tmp_pool.give_back(th, [m])
                    h.append(cell)
                    tiles.append(m)
                xnt_pool.give_back(xnt, [m2])
                for key, scale in (("h1_t", sh1), ("h2_t", sh2)):
                    w_ok = (yield ("read", key)) + (yield ("read", "s" + key[0:2]))
                    new, new_tiles = [], []
                    for mt in range(MT):
                        bank, free = yield ("take", banks)

                        def layer(e, k, bank=bank):
                            for i in range(PARTS):
                                c = k * HID + mt * P
                                ins = e.matmul(bank[:], w[key][:, c:c + P], h[k][:, i],
                                               start=(k + i == 0), stop=(k == MT - 1 and i == PARTS - 1))
                            return ins
                        for k in range(MT):
                            m = yield step("tensor", pe_cost(512, passes), "F", lambda e: layer(e, k),
                                           tiles[k * PARTS:(k + 1) * PARTS] + (w_ok + free if k == 0 else []))
                        cell, cell_free = yield ("take", hid_pool)
                        if general:
                            a = yield step("scalar", act_cost(512, True, 1), "F", lambda e, bank=bank: e.activation(
                                cell[:, 0], bank[:], ACT.Gelu, scale=scale[:, mt:mt + 1]), [m] + cell_free)
                            banks.give_back(bank, [a])
                        else:
                            full, full_free = yield ("take", tmp_pool)
                            a = yield step("scalar", act_cost(512, True, 1), "F", lambda e, bank=bank: e.activation(
                                full[:], bank[:], ACT.Gelu, scale=scale[:, mt:mt + 1]), [m] + full_free)
                            banks.give_back(bank, [a])
                            hi = yield step("vector", dve_cost(512, True), "F", lambda e: e.tensor_copy(
                                cell[:, 0], full[:]), [a] + cell_free)
                            a = yield low_part(cell, full[:], "gpsimd" if mt % 2 else "vector", [hi])
                            tmp_pool.give_back(full, [a])
                            new_tiles.append(hi)
                        new.append(cell)
                        new_tiles.append(a)
                    for cell in h:
                        hid_pool.give_back(cell, [m])
                    h, tiles = new, new_tiles
                board["f_last_layer", b] = True
                w_ok = (yield ("read", "w3_t")) + (yield ("read", "s3_row"))
                bank, free = yield ("take", banks)

                def down(e):
                    for k in range(NT):
                        for mt in range(MT):
                            for i in range(PARTS):
                                ins = e.matmul(bank[:, k * P:(k + 1) * P], h[mt][:, i, k * P:(k + 1) * P],
                                               w["w3_t"][:, mt * DM:(mt + 1) * DM],
                                               start=(mt + i == 0), stop=(mt == MT - 1 and i == PARTS - 1))
                    return ins
                m = yield step("tensor", pe_cost(2048, passes), "F", down, tiles + w_ok + free)
                for cell in h:
                    hid_pool.give_back(cell, [m])
                (slot, out), o_free = yield ("take", out_pool)
                m = yield step("vector", dve_cost(512), "F", lambda e: e.tensor_tensor(
                    out[:], bank[:].rearrange("p (k f) -> p k f", k=NT),
                    s3_row[:].unsqueeze(1).to_broadcast([P, NT, DM]), ALU.mult), [m] + w_ok + o_free)
                banks.give_back(bank, [m])
                s = slice(b * NT, b * NT + NT)
                m = yield step("vector", dve_cost(512), "F", lambda e: e.tensor_tensor(
                    out[:], out[:], x_res[:, s], ALU.add), [m])
                m = yield step("sync", 2500, "F", lambda e: e.dma_start(t["out"][:, s], out[:]), [m], f"store{slot}")
                out_pool.give_back((slot, out), [m])
                board["f_done", b] = True

            def f_flags():
                yield ("read", ("f_done", NSEQ - 1))
                m = yield step("vector", 90, "F", lambda e: e.tensor_reduce(flags[:, 0:1], kept_max[:], AX, ALU.max), [])
                bank, free = yield ("take", banks)
                m = yield step("tensor", 200, "F", lambda e: e.matmul(
                    bank[:, 0:3], ones[:], flags[:], start=True, stop=True), [m, (yield ("read", "f_unequal"))] + free)
                kept = yield step("vector", 90, "F", lambda e: e.tensor_scalar(
                    kept_sum[:], bank[:, 0:1], 0.0, None, ALU.is_gt), [m])
                yield step("vector", 90, "F", lambda e: e.tensor_scalar(
                    kept_thr[:, 0:1], kept_sum[:], 1.0 + 1.0 / NE, -1.0, ALU.mult, ALU.add), [kept])
                yield step("vector", 90, "F", lambda e: e.tensor_scalar(
                    kept_thr[:, 1:2], kept_sum[:], TOP_K - 1.0, 0.5, ALU.mult, ALU.add), [kept])
                m = yield step("vector", 90, "F", lambda e: e.tensor_reduce(
                    flags[0:1, 1:2], bank[0:1, 1:3], AX, ALU.add), [m])
                m = yield step("vector", 90, "F", lambda e: e.scalar_tensor_tensor(
                    out=go_on[:], in0=flags[0:1, 1:2], scalar=0.0, in1=kept_sum[0:1], op0=ALU.is_equal,
                    op1=ALU.mult), [kept, m])
                banks.give_back(bank, [m])
                board["go_on"] = m

            weave(mc, [(0, tables(TABLES_GELU))])
            strands = [(0, f_weights())] + [(b + 1, f_all(b)) for b in range(NSEQ)]
            if not general:
                strands += [(NSEQ + 1, f_compare()), (NSEQ + 2, f_flags())]
            weave(mc, strands)

        def tables(which):
            yield step("scalar", 1300, "init", lambda e: e.add_instruction(mybir.InstLoadActFuncSet(
                name=nc.get_next_instruction_name(), act_func_set_id=which)), [])

        def one_pass(tag, general):
            board.clear()
            with ExitStack() as area:
                phase_one(area, tag + "_1", general)
            mc.join(("load_",))
            if "F" in stages:
                with ExitStack() as area:
                    phase_two(area, tag + "_2", general)
            else:
                nc.sync.dma_start(t["out"], x_res[:]).then_inc(mc.sem("store"), 16)
                mc.count["store"] += 16
            for name in mc.sems:
                if name.startswith(("load_", "stack", "rows", "store")):
                    nc.sync.wait_ge(mc.sems[name], mc.count[name])

        one_pass("fast", False)
        if "F" in stages:
            go_on_ok = board["go_on"]
            for eng in mc.engines.values():
                eng.wait_ge(mc.sems[go_on_ok.sem], go_on_ok.value)
            held = nc.values_load(go_on[0:1, 0:1], min_val=0, max_val=1)
            with nc.If(held == 0):
                mc.join(())
                one_pass("general", True)


def layouts(i):
    c = np.ascontiguousarray
    chan = lambda a: c(a.reshape(CT, P, -1).transpose(1, 0, 2))
    tiles = lambda a: c(a.reshape(MT, P).T)
    rows_k = lambda a: c(a.T.reshape(MT, P, -1).transpose(1, 0, 2))
    swap = np.arange(HEADS * DR) ^ 1
    g = {
        "x": c(i["L0_attn_x"].reshape(NSEQ * NT, P, DM).transpose(1, 0, 2)),
        "w_in": c(i["L0_attn_W_in"].T),
        "conv_w": chan(i["L0_attn_conv_w"]),
        "conv_b": c(i["L0_attn_conv_b"].reshape(CT, P).T),
        "a_log": c(chan(i["L0_attn_A_log"]).reshape(P, CT * STATE)),
        "skip_d": c(i["L0_attn_D"].reshape(CT, P).T),
        "w_out": c(i["L0_attn_W_out"].T.reshape(CT, P, DM).transpose(1, 0, 2)),
        "vg_t": c(i["L0_ffn_Vg"].transpose(2, 0, 1).reshape(GATE_K, NE * P)),
        "we_t": c(i["L0_ffn_We"].transpose(2, 0, 1).reshape(P, NE * P)),
        "wp_t": c(i["L0_ffn_Wp"].T),
        "bias_e": c(np.concatenate([i["L0_ffn_be"], i["L0_ffn_bp"][None]])),
        "lat_w": c(np.concatenate([i["L1_attn_W_DQ"], i["L1_attn_W_DKV"]], 1)),
        "kr_w": c(np.concatenate([i["L1_attn_W_KR"], i["L1_attn_W_KR"][:, swap[:DR]]], 1)),
        "up_w": c(np.concatenate([
            np.concatenate([i["L1_attn_W_UQ"], i["L1_attn_W_QR"], i["L1_attn_W_QR"][:, swap]], 1),
            np.concatenate([i["L1_attn_W_UK"], i["L1_attn_W_UV"]], 1)], 0)),
        "w_o": c(i["L1_attn_W_O"]),
        "w1_t": c(i["L1_ffn_w1_w"].T), "w2_t": c(i["L1_ffn_w2_w"].T),
        "h1_t": rows_k(i["L1_ffn_h1_w"]), "h2_t": rows_k(i["L1_ffn_h2_w"]), "w3_t": rows_k(i["L1_ffn_w3_w"]),
        "s1": tiles(i["L1_ffn_w1_s"]), "s2": tiles(i["L1_ffn_w2_s"]),
        "sh1": tiles(i["L1_ffn_h1_s"]), "sh2": tiles(i["L1_ffn_h2_s"]),
        "s3_row": c(np.broadcast_to(i["L1_ffn_w3_s"], (P, DM))),
    }
    sel = np.zeros((P, 2, 32), np.float32)
    p = np.arange(P)
    sel[p, 0, p // DH] = 1
    sel[p[:HEADS * DR], 1, p[:HEADS * DR] // DR] = 1
    sel[HEADS * DR:HEADS * DR + DR, 1, 0:HEADS] = 1
    g["sel"] = sel.reshape(P, 64)
    g["ident"] = np.eye(P, dtype=np.float32)
    inv = np.float32(10000.0) ** (-np.arange(0, DR, 2, dtype=np.float32) / np.float32(DR))
    ang = np.arange(SEQ, dtype=np.float32)[:, None] * inv.astype(np.float32)
    cos, sin = np.cos(ang).astype(np.float32).T, np.sin(ang).astype(np.float32).T
    d = np.arange(HEADS * DR + DR) % DR
    g["rope"] = c(np.stack([cos[d // 2], np.where((d % 2 == 0)[:, None], -sin[d // 2], sin[d // 2])], 1))
    e, j = np.arange(NE)[:, None], np.arange(NE)[None, :]
    g["tie"] = c(np.broadcast_to(np.where(j < e, np.float32(-1e-30), np.float32(0.0)), (P, NE, NE)))
    return g


STAGES = "SGTF"


def kernel(**inputs):
    import concourse.bacc as _bacc
    from concourse.bass_utils import run_bass_kernel_spmd as _run

    nc = _bacc.Bacc("TRN2", target_bir_lowering=False, num_devices=1)
    arrays = {f"in_{k}": v for k, v in layouts({k: np.asarray(v) for k, v in inputs.items()}).items()}
    t = {k[3:]: nc.dram_tensor(k, v.shape, mybir.dt.from_np(v.dtype), kind="ExternalInput").ap()
         for k, v in arrays.items()}
    for name in ("q_rows", "k_rows"):
        t[name] = nc.dram_tensor(name, (NSEQ, HEADS, 3 * DQK, SEQ), BF16, kind="Internal").ap()
    t["out"] = nc.dram_tensor("out_x", (P, NSEQ * NT, DM), F32, kind="ExternalOutput").ap()
    build(nc, t, STAGES)
    r = _run(nc, [arrays], core_ids=[0])
    out = r.results[0]["out_x"]
    return np.ascontiguousarray(np.asarray(out).transpose(1, 0, 2).reshape(NSEQ, SEQ, DM))
```
